# Optimizing a Trainium2 kernel written in Bass

```python
import numpy as np
import jax
import jax.numpy as jnp

def _softmax(x, axis=-1):
    return jax.nn.softmax(x, axis=axis)

def _gelu(x):
    return jax.nn.gelu(x, approximate=True)

def _silu(x):
    return jax.nn.silu(x)

def _sigmoid(x):
    return jax.nn.sigmoid(x)

def _layernorm(x, axis=-1, eps=1e-05):
    m = jnp.mean(x, axis=axis, keepdims=True)
    v = jnp.var(x, axis=axis, keepdims=True)
    return (x - m) / jnp.sqrt(v + eps)

def _scatter_add(tgt, idx, src, axis=0):
    return tgt.at[idx].add(src)

def _segment_sum(src, seg, n):
    return jax.ops.segment_sum(src, seg, n)
kernel_name = 'mk_dlrm_tower_d1_rec_r8_d4836e'

def setup_inputs(seed: int=0):
    np.random.seed(seed)
    _w = jnp.asarray

    def _rec_inputs():
        import jax
        import jax.numpy as jnp
        _tk = jax.random.key(seed)
        dense_ctx = jax.random.normal(jax.random.fold_in(_tk, 190), (512, 16), jnp.float32)
        ids = jnp.stack([jax.random.randint(jax.random.fold_in(_tk, 200 + f), (512,), 0, v, jnp.int32) for f, v in enumerate([1000, 12500, 125000, 12500, 1250, 12500, 1250, 12500, 1250, 1000, 12500, 1000, 12500, 1000, 12500, 125000, 12500, 1250, 12500, 1000, 1000, 12500, 1250, 1250, 12500, 1250, 12500, 12500, 12500, 12500, 1000, 1250])], axis=1)
        tbl_0 = 0.05 * jax.random.normal(jax.random.fold_in(_tk, 500 + 0), (1000, 64), jnp.float32)
        tbl_1 = 0.05 * jax.random.normal(jax.random.fold_in(_tk, 500 + 1), (12500, 64), jnp.float32)
        tbl_2 = 0.05 * jax.random.normal(jax.random.fold_in(_tk, 500 + 2), (125000, 64), jnp.float32)
        tbl_3 = 0.05 * jax.random.normal(jax.random.fold_in(_tk, 500 + 3), (12500, 64), jnp.float32)
        tbl_4 = 0.05 * jax.random.normal(jax.random.fold_in(_tk, 500 + 4), (1250, 64), jnp.float32)
        tbl_5 = 0.05 * jax.random.normal(jax.random.fold_in(_tk, 500 + 5), (12500, 64), jnp.float32)
        tbl_6 = 0.05 * jax.random.normal(jax.random.fold_in(_tk, 500 + 6), (1250, 64), jnp.float32)
        tbl_7 = 0.05 * jax.random.normal(jax.random.fold_in(_tk, 500 + 7), (12500, 64), jnp.float32)
        tbl_8 = 0.05 * jax.random.normal(jax.random.fold_in(_tk, 500 + 8), (1250, 64), jnp.float32)
        tbl_9 = 0.05 * jax.random.normal(jax.random.fold_in(_tk, 500 + 9), (1000, 64), jnp.float32)
        tbl_10 = 0.05 * jax.random.normal(jax.random.fold_in(_tk, 500 + 10), (12500, 64), jnp.float32)
        tbl_11 = 0.05 * jax.random.normal(jax.random.fold_in(_tk, 500 + 11), (1000, 64), jnp.float32)
        tbl_12 = 0.05 * jax.random.normal(jax.random.fold_in(_tk, 500 + 12), (12500, 64), jnp.float32)
        tbl_13 = 0.05 * jax.random.normal(jax.random.fold_in(_tk, 500 + 13), (1000, 64), jnp.float32)
        tbl_14 = 0.05 * jax.random.normal(jax.random.fold_in(_tk, 500 + 14), (12500, 64), jnp.float32)
        tbl_15 = 0.05 * jax.random.normal(jax.random.fold_in(_tk, 500 + 15), (125000, 64), jnp.float32)
        tbl_16 = 0.05 * jax.random.normal(jax.random.fold_in(_tk, 500 + 16), (12500, 64), jnp.float32)
        tbl_17 = 0.05 * jax.random.normal(jax.random.fold_in(_tk, 500 + 17), (1250, 64), jnp.float32)
        tbl_18 = 0.05 * jax.random.normal(jax.random.fold_in(_tk, 500 + 18), (12500, 64), jnp.float32)
        tbl_19 = 0.05 * jax.random.normal(jax.random.fold_in(_tk, 500 + 19), (1000, 64), jnp.float32)
        tbl_20 = 0.05 * jax.random.normal(jax.random.fold_in(_tk, 500 + 20), (1000, 64), jnp.float32)
        tbl_21 = 0.05 * jax.random.normal(jax.random.fold_in(_tk, 500 + 21), (12500, 64), jnp.float32)
        tbl_22 = 0.05 * jax.random.normal(jax.random.fold_in(_tk, 500 + 22), (1250, 64), jnp.float32)
        tbl_23 = 0.05 * jax.random.normal(jax.random.fold_in(_tk, 500 + 23), (1250, 64), jnp.float32)
        tbl_24 = 0.05 * jax.random.normal(jax.random.fold_in(_tk, 500 + 24), (12500, 64), jnp.float32)
        tbl_25 = 0.05 * jax.random.normal(jax.random.fold_in(_tk, 500 + 25), (1250, 64), jnp.float32)
        tbl_26 = 0.05 * jax.random.normal(jax.random.fold_in(_tk, 500 + 26), (12500, 64), jnp.float32)
        tbl_27 = 0.05 * jax.random.normal(jax.random.fold_in(_tk, 500 + 27), (12500, 64), jnp.float32)
        tbl_28 = 0.05 * jax.random.normal(jax.random.fold_in(_tk, 500 + 28), (12500, 64), jnp.float32)
        tbl_29 = 0.05 * jax.random.normal(jax.random.fold_in(_tk, 500 + 29), (12500, 64), jnp.float32)
        tbl_30 = 0.05 * jax.random.normal(jax.random.fold_in(_tk, 500 + 30), (1000, 64), jnp.float32)
        tbl_31 = 0.05 * jax.random.normal(jax.random.fold_in(_tk, 500 + 31), (1250, 64), jnp.float32)
        _rk = jax.random.fold_in(_tk, 7)
        W_top1 = 0.0441942 * jax.random.normal(jax.random.fold_in(_tk, 801), (512, 512), jnp.float32)
        W_top2 = 0.0441942 * jax.random.normal(jax.random.fold_in(_tk, 802), (512, 256), jnp.float32)
        W_top3 = 0.0625 * jax.random.normal(jax.random.fold_in(_tk, 803), (256, 1), jnp.float32)
        b_top1 = jnp.zeros((512,), jnp.float32)
        b_top2 = jnp.zeros((256,), jnp.float32)
        return (dense_ctx, ids, tbl_0, tbl_1, tbl_2, tbl_3, tbl_4, tbl_5, tbl_6, tbl_7, tbl_8, tbl_9, tbl_10, tbl_11, tbl_12, tbl_13, tbl_14, tbl_15, tbl_16, tbl_17, tbl_18, tbl_19, tbl_20, tbl_21, tbl_22, tbl_23, tbl_24, tbl_25, tbl_26, tbl_27, tbl_28, tbl_29, tbl_30, tbl_31, W_top1, b_top1, W_top2, b_top2, W_top3)
    dense_ctx, ids, tbl_0, tbl_1, tbl_2, tbl_3, tbl_4, tbl_5, tbl_6, tbl_7, tbl_8, tbl_9, tbl_10, tbl_11, tbl_12, tbl_13, tbl_14, tbl_15, tbl_16, tbl_17, tbl_18, tbl_19, tbl_20, tbl_21, tbl_22, tbl_23, tbl_24, tbl_25, tbl_26, tbl_27, tbl_28, tbl_29, tbl_30, tbl_31, W_top1, b_top1, W_top2, b_top2, W_top3 = _rec_inputs()

    def _L0_rec_setup():
        import jax, jax.numpy as jnp
        import numpy as np
        FIELDS = 32
        EMBED = 64
        BATCH = 1024
        PAIR = FIELDS * (FIELDS - 1) // 2

        def _pair_ids(fields):
            pairs = np.array([(i, j) for i in range(fields - 1) for j in range(i + 1, fields)], dtype=np.int32)
            return (jnp.asarray(pairs[:, 0]), jnp.asarray(pairs[:, 1]))
        key = jax.random.key(seed)
        k1, k2 = jax.random.split(key)
        inputs = jax.random.normal(k1, (BATCH, FIELDS, EMBED), dtype=jnp.float32)
        w = 0.05 * jax.random.normal(k2, (PAIR, EMBED, EMBED), dtype=jnp.float32)
        return {'inputs': inputs, 'w': w}
    _L0_rec_all = _L0_rec_setup()
    _L0_rec_in = {k: v for k, v in _L0_rec_all.items() if k in ('w',)}
    del _L0_rec_all
    return {'dense_ctx': dense_ctx, 'ids': ids, 'tbl_0': tbl_0, 'tbl_1': tbl_1, 'tbl_2': tbl_2, 'tbl_3': tbl_3, 'tbl_4': tbl_4, 'tbl_5': tbl_5, 'tbl_6': tbl_6, 'tbl_7': tbl_7, 'tbl_8': tbl_8, 'tbl_9': tbl_9, 'tbl_10': tbl_10, 'tbl_11': tbl_11, 'tbl_12': tbl_12, 'tbl_13': tbl_13, 'tbl_14': tbl_14, 'tbl_15': tbl_15, 'tbl_16': tbl_16, 'tbl_17': tbl_17, 'tbl_18': tbl_18, 'tbl_19': tbl_19, 'tbl_20': tbl_20, 'tbl_21': tbl_21, 'tbl_22': tbl_22, 'tbl_23': tbl_23, 'tbl_24': tbl_24, 'tbl_25': tbl_25, 'tbl_26': tbl_26, 'tbl_27': tbl_27, 'tbl_28': tbl_28, 'tbl_29': tbl_29, 'tbl_30': tbl_30, 'tbl_31': tbl_31, 'W_top1': W_top1, 'b_top1': b_top1, 'W_top2': W_top2, 'b_top2': b_top2, 'W_top3': W_top3, 'L0_rec_w': _L0_rec_in['w']}

def reference(dense_ctx, ids, tbl_0, tbl_1, tbl_2, tbl_3, tbl_4, tbl_5, tbl_6, tbl_7, tbl_8, tbl_9, tbl_10, tbl_11, tbl_12, tbl_13, tbl_14, tbl_15, tbl_16, tbl_17, tbl_18, tbl_19, tbl_20, tbl_21, tbl_22, tbl_23, tbl_24, tbl_25, tbl_26, tbl_27, tbl_28, tbl_29, tbl_30, tbl_31, W_top1, b_top1, W_top2, b_top2, W_top3, L0_rec_w):
    import jax
    import jax.numpy as jnp

    def _L0_rec_ref(inputs, w):
        import jax, jax.numpy as jnp
        import numpy as np
        FIELDS = 32
        EMBED = 64
        BATCH = 1024
        PAIR = FIELDS * (FIELDS - 1) // 2

        def _pair_ids(fields):
            pairs = np.array([(i, j) for i in range(fields - 1) for j in range(i + 1, fields)], dtype=np.int32)
            return (jnp.asarray(pairs[:, 0]), jnp.asarray(pairs[:, 1]))
        ids_x, ids_y = _pair_ids(FIELDS)
        p = inputs[:, ids_x, :]
        q = inputs[:, ids_y, :]
        pw = jnp.einsum('bpi,pij->bpj', p, w)
        out = jnp.einsum('bpj,bpj->bp', pw, q)
        return out
    e = jnp.stack([tbl_0[ids[:, 0]], tbl_1[ids[:, 1]], tbl_2[ids[:, 2]], tbl_3[ids[:, 3]], tbl_4[ids[:, 4]], tbl_5[ids[:, 5]], tbl_6[ids[:, 6]], tbl_7[ids[:, 7]], tbl_8[ids[:, 8]], tbl_9[ids[:, 9]], tbl_10[ids[:, 10]], tbl_11[ids[:, 11]], tbl_12[ids[:, 12]], tbl_13[ids[:, 13]], tbl_14[ids[:, 14]], tbl_15[ids[:, 15]], tbl_16[ids[:, 16]], tbl_17[ids[:, 17]], tbl_18[ids[:, 18]], tbl_19[ids[:, 19]], tbl_20[ids[:, 20]], tbl_21[ids[:, 21]], tbl_22[ids[:, 22]], tbl_23[ids[:, 23]], tbl_24[ids[:, 24]], tbl_25[ids[:, 25]], tbl_26[ids[:, 26]], tbl_27[ids[:, 27]], tbl_28[ids[:, 28]], tbl_29[ids[:, 29]], tbl_30[ids[:, 30]], tbl_31[ids[:, 31]]], axis=1)
    z = _L0_rec_ref(e, L0_rec_w)
    z = z.reshape(z.shape[0], -1)
    h = jnp.concatenate([z, dense_ctx], axis=1)
    h = jnp.maximum(h @ W_top1 + b_top1, 0.0)
    h = jnp.maximum(h @ W_top2 + b_top2, 0.0)
    y = h @ W_top3
    return y

_drawn_inputs = setup_inputs


def setup_inputs(seed=0):
    import zlib

    import numpy as np

    out = dict(_drawn_inputs(seed))
    spreads = {'b_top1': (0.0, 0.1), 'b_top2': (0.0, 0.1)}
    factors = {'tbl_0': 6.631,
     'tbl_1': 6.319,
     'tbl_2': 5.561,
     'tbl_3': 5.692,
     'tbl_4': 4.954,
     'tbl_5': 6.363,
     'tbl_6': 5.49,
     'tbl_7': 5.175,
     'tbl_8': 5.529,
     'tbl_9': 5.562,
     'tbl_10': 5.671,
     'tbl_11': 5.53,
     'tbl_12': 5.414,
     'tbl_13': 5.264,
     'tbl_14': 5.683,
     'tbl_15': 5.71,
     'tbl_16': 5.288,
     'tbl_17': 5.774,
     'tbl_18': 5.439,
     'tbl_19': 5.715,
     'tbl_20': 5.485,
     'tbl_21': 5.795,
     'tbl_22': 5.849,
     'tbl_23': 6.324,
     'tbl_24': 5.441,
     'tbl_25': 5.425,
     'tbl_26': 5.735,
     'tbl_27': 5.973,
     'tbl_28': 6.03,
     'tbl_29': 5.658,
     'tbl_30': 5.541,
     'tbl_31': 6.091}
    for name, (base, spread) in spreads.items():
        noise = np.random.default_rng([zlib.crc32(name.encode()), seed]).standard_normal(out[name].shape)
        drawn = base * np.exp(spread * noise) if base else spread * noise
        out[name] = jnp.asarray(drawn.astype(out[name].dtype))
    for name, factor in factors.items():
        out[name] = (out[name] * factor).astype(out[name].dtype)
    return out
```

```python
from contextlib import ExitStack

import concourse.bass as bass
from concourse import mybir

F32 = mybir.dt.float32
F32R = mybir.dt.float32r
BF16 = mybir.dt.bfloat16
I32 = mybir.dt.int32
ALU = mybir.AluOpType
ACT = mybir.ActivationFunctionType

P = 128
FIELDS = 32
EMBED = 64
BATCH = 512
BT = BATCH // P
MS = FIELDS // 2
GS = FIELDS // 4
DENSE = 16
N1, N2 = 512, 256
SPLIT_RING = 3
SLOTS = 4
PRODUCT_RING = 8
GATHER_RING = 4
POOL_SPLITS_FROM = 8
SUM_LAG = 4
SPLIT_AHEAD = 2


def pair(i, j):
    return i * (FIELDS - 1) - i * (i - 1) // 2 + j - i - 1


def lane_of(i, m):
    before = sum(2 * (MS - 1 - a // 2) for a in range(i % 4, i, 4))
    return before + 2 * (m - i // 2 - 1)


def chunks_of(m):
    return (2 * m + 3) // 4


def first_chunk(m):
    return sum(chunks_of(a) for a in range(m))


def chunk_list():
    return [(m, c) for m in range(MS) for c in range(chunks_of(m))]


def schedule():
    GATHER, POOL_SPLIT, BLOCK, TRANSPOSES, LANDING = 3.1, 3.7, 2, 4, 6
    chunks = chunk_list()
    gathers = [(m, f, t) for m in range(MS) for f in range(2) for t in range(BT)]
    steps, landed = [], {}
    pool = tensor = 0
    gathered = split = taken = 0
    parts_age = None

    def gather_until(limit):
        nonlocal pool, gathered
        while gathered < len(gathers) and gathers[gathered][0] < taken + GATHER_RING and pool < limit:
            steps.append(("gather", *gathers[gathered]))
            pool += GATHER
            landed[gathers[gathered][0]] = pool + LANDING
            gathered += 1

    def split_chunk():
        nonlocal pool, split
        if split < len(chunks):
            if chunks[split][0] >= POOL_SPLITS_FROM:
                gather_until(tensor)
                pool = max(pool, tensor) + POOL_SPLIT
            steps.append(("weights", split))
            split += 1

    def take_fields(now):
        nonlocal tensor, taken, parts_age
        if taken == MS:
            return
        if now:
            gather_until(float("inf") if gathered < 8 * (taken + 1) else tensor)
            tensor = max(tensor, landed[taken])
        if parts_age is None and gathered >= 8 * (taken + 1) and tensor >= landed[taken]:
            steps.append(("parts", taken))
            parts_age = 0
        if parts_age is not None and (now or parts_age >= 3):
            steps.append(("transposes", taken))
            tensor += TRANSPOSES
            taken += 1
            parts_age = None

    steps.append(("diagonals", 0))
    for _ in range(SPLIT_AHEAD):
        split_chunk()
    for m in range(MS):
        if taken == m:
            take_fields(True)
        gather_until(tensor)
        steps.append(("diagonal", m))
        if m % 2 and m // 2 + 1 < GS:
            steps.append(("diagonals", m // 2 + 1))
        for i in range(2 * m):
            steps.append(("block", m, i))
            tensor += BLOCK
            if parts_age is not None:
                parts_age += 1
            if i % 4 == 0:
                split_chunk()
            gather_until(tensor)
            take_fields(False)
    assert taken == MS and gathered == len(gathers) and split == len(chunks)
    return steps


def dlrm_tower(nc, dense_ctx, ids, tables, W_top1, b_top1, W_top2, b_top2, W_top3, w, out):
    STEPS = schedule()
    slot_at = {}
    product_at = {}
    split_at = {}
    for s in STEPS:
        if s[0] == "transposes":
            for f in range(min(2, FIELDS - 1 - 2 * s[1])):
                slot_at["T", s[1], f] = len(slot_at)
            slot_at["E", s[1]] = len(slot_at)
        elif s[0] == "diagonal":
            slot_at["D", s[1]] = len(slot_at)
        elif s[0] == "block":
            slot_at[s[1:]] = len(slot_at)
            product_at[s[1:]] = len(product_at)
        elif s[0] in ("weights", "diagonals"):
            split_at[s] = len(split_at)
    by_slot = {n: k for k, n in slot_at.items()}
    BLOCKS = len(product_at)
    block_of = {n: k for k, n in product_at.items()}
    chunks = chunk_list()
    def loads_of(g, c):
        return sum(5 if c < a else 6 for a in range(g % 2, g + 1, 2) if c <= a)

    def by_pool(step):
        return step[0] == "weights" and chunks[step[1]][0] >= POOL_SPLITS_FROM

    low_at = {}
    for s in STEPS:
        if s in split_at:
            low_at[s] = sum(by_pool(a) == by_pool(s) for a in low_at)

    with ExitStack() as ctx:
        def sb(name, shape, dt=F32):
            return ctx.enter_context(nc.sbuf_tensor(name, shape, dt))

        def sem(name):
            return ctx.enter_context(nc.semaphore(name))

        ids_sb = sb("ids_sb", [P, BT, FIELDS], I32)
        gathered = sb("gathered", [P, GATHER_RING, BT, 2, EMBED])
        parts = sb("parts", [P, 2, BT, 2, 2, EMBED])
        e_parts = sb("e_parts", [P, FIELDS - 1, BATCH], F32R)
        e_pairs = sb("e_pairs", [P, MS, BATCH])
        raw_rows = [4 * (GS - 1), 4 * GS]
        raw = [sb(f"raw{h}", [P, raw_rows[h], 4, EMBED]) for h in range(2)]
        w_high = sb("w_high", [P, SPLIT_RING, 4, 2 * EMBED], F32R)
        w_low = sb("w_low", [P, SPLIT_RING, 4, 2 * EMBED], F32R)
        d_high = sb("d_high", [P, 2, 2, 2, EMBED], F32R)
        d_low = sb("d_low", [P, 2, 2, 2, EMBED], F32R)
        products = sb("products", [P, PRODUCT_RING, BATCH])
        d_products = sb("d_products", [P, BATCH])
        selector = sb("selector", [P, 2 * 32])
        identity = sb("identity", [P, P])
        zero_row = sb("zero_row", [1, BATCH], BF16)
        dense_sb = sb("dense_sb", [P, BT, 32])
        b1_sb = sb("b1_sb", [P, N1 // P])
        b2_sb = sb("b2_sb", [P, N2 // P])
        w3_sb = sb("w3_sb", [P, N2 // P])

        tail = raw[0][:].rearrange("p i j l -> p (i j l)")
        w1_sb = tail[:, 0:4 * N1].rearrange("p (t n) -> p t n", t=4)
        w2_sb = tail[:, 4 * N1:4 * N1 + 4 * N2].rearrange("p (t n) -> p t n", t=4)
        z_sb = tail[:, 3072:3072 + 4 * BATCH].rearrange("p (t b) -> p t b", t=4)
        h1_sb = tail[:, 5120:5120 + 4 * BATCH].rearrange("p (t b) -> p t b", t=4)
        h2_sb = e_pairs[:, 0:2, :]
        y_sb = e_pairs[0:1, 2, :]

        z_ps = ctx.enter_context(nc.psum_tensor("z_ps", [P, 4, BATCH], F32))
        slots = ctx.enter_context(nc.psum_tensor("slots", [P, SLOTS, BATCH], F32))

        ids_loaded = sem("ids_loaded")
        small_loaded = sem("small_loaded")
        w1_loaded = sem("w1_loaded")
        raw_loaded = [[sem(f"raw{h}_rows{4 * c}_loaded") for c in range(GS)] for h in range(2)]
        fields_gathered = [sem(f"fields_gathered{h}") for h in range(GATHER_RING)]
        constants_ready = sem("constants_ready")
        identity_ready = sem("identity_ready")
        dense_cleared = sem("dense_cleared")
        parts_high = sem("parts_high")
        parts_ready = sem("parts_ready")
        w_high_ready = sem("w_high_ready")
        w_low_vector = sem("w_low_vector")
        w_low_pool = sem("w_low_pool")
        slot_filled = sem("slot_filled")
        slot_copied = sem("slot_copied")
        products_ready = sem("products_ready")
        diagonals_ready = sem("diagonals_ready")
        diagonals_summed = sem("diagonals_summed")
        products_summed = sem("products_summed")
        z_copied = [sem("z_copied_act"), sem("z_copied_dve")]
        h1_filled = sem("h1_filled")
        h1_ready = [sem("h1_ready_act"), sem("h1_ready_dve")]
        h2_filled = sem("h2_filled")
        h2_ready = [sem("h2_ready_act"), sem("h2_ready_dve")]
        y_filled = sem("y_filled")
        y_ready = sem("y_ready")
        y_stored = sem("y_stored")

        def wait_split(engine, *step):
            engine.wait_ge(w_low_pool if by_pool(step) else w_low_vector, low_at[step] + 1)

        def wait_rows_split(engine, g, c):
            if c < chunks_of(2 * g + 1):
                wait_split(engine, "weights", first_chunk(2 * g + 1) + c)
            if c == g:
                wait_split(engine, "diagonals", g)

        def wait_group_split(engine, g):
            wait_rows_split(engine, g, g)

        def copies_before(n):
            return sum(by_slot[a][0] in ("T", "E") for a in range(n))

        def raw_chunk(m, c):
            g = m // 2
            rows = min(4, 2 * m - 4 * c)
            j = 2 * (m % 2)
            return raw[g % 2][:, 4 * c:4 * c + rows, j:j + 2, :], rows

        def raw_diagonals(g):
            flat = raw[g % 2][:].rearrange("p i j l -> p (i j) l")
            return flat[:, 16 * g + 1:16 * g + 12:10, :]

        W1_LOADS = 2 + MS + sum(
            1 + (lane_of(i, MS - 1) + 1) // 32 - lane_of(i, i // 2 + 1) // 32 for i in range(FIELDS - 2))

        def low_part(engine, c):
            src, rows = raw_chunk(*chunks[c])
            low, high = (x[:, c % SPLIT_RING, 0:rows, :].rearrange("p i (j l) -> p i j l", j=2)
                         for x in (w_low, w_high[:].bitcast(F32)))
            return engine.tensor_tensor(low, src, high, ALU.subtract)

        block = ctx.enter_context(nc.Block())

        @block.sync
        def _(sp):
            sp.dma_start(ids_sb[:], ids.rearrange("(t p) f -> p t f", p=P)).then_inc(ids_loaded, 16)

            def load_raw(g, c):
                for i in range(4 * c, min(4 * c + 4, 4 * g + 3)):
                    j = max(4 * g, i + 1)
                    k = 4 * g + 4 - j
                    src = w[pair(i, j):pair(i, j) + k, :, :].rearrange("p k l -> k p l")
                    for half in range(1 if c < g else 2):
                        sp.dma_start(raw[g % 2][64 * half:64 * half + 64, i, 4 - k:4, :], src
                                     ).then_inc(raw_loaded[g % 2][c], 16)

            def copy_raw(g, c):
                if c < g:
                    sp.wait_ge(raw_loaded[g % 2][c], 16 * (loads_of(g, c) - 1))
                    sp.dma_start(raw[g % 2][64:128, 4 * c:4 * c + 4, :, :],
                                 raw[g % 2][0:64, 4 * c:4 * c + 4, :, :]).then_inc(raw_loaded[g % 2][c], 16)

            before = None
            for g in range(GS):
                for c in range(g + 1):
                    if g >= 2 and c < g - 1:
                        wait_rows_split(sp, g - 2, c)
                    load_raw(g, c)
                    if before:
                        copy_raw(*before)
                    before = g, c

            wait_group_split(sp, GS - 2)
            sp.dma_start(w2_sb, W_top2.rearrange("(t p) n -> p t n", p=P)).then_inc(w1_loaded, 16)
            n = 1
            for i in range(FIELDS - 2):
                lane, row, left = lane_of(i, i // 2 + 1), pair(i, 2 * (i // 2 + 1)), 2 * (MS - 1 - i // 2)
                while left:
                    t, r = lane // 32, lane % 32
                    k = min(left, 32 - r)
                    at = 32 * (i % 4) + r
                    sp.dma_start(w1_sb[at:at + k, t, :], W_top1[row:row + k, :]).then_inc(w1_loaded, 16)
                    lane, row, left, n = lane + k, row + k, left - k, n + 1
            for m in range(MS):
                row = pair(2 * m, 2 * m + 1)
                sp.dma_start(w1_sb[80 + m:81 + m, 3, :], W_top1[row:row + 1, :]).then_inc(w1_loaded, 16)
            sp.dma_start(w1_sb[112:128, 3, :], W_top1[N1 - DENSE:N1, :]).then_inc(w1_loaded, 16)
            assert n + MS + 1 == W1_LOADS
            sp.wait_ge(y_ready, 1)
            sp.dma_start(out.rearrange("b o -> o b"), y_sb).then_inc(y_stored, 16)
            sp.wait_ge(y_stored, 16)

        @block.gpsimd
        def _(pool):
            pool.wait_ge(constants_ready, 3)
            pool.affine_select(out=identity[:], in_=identity[:], compare_op=ALU.not_equal, fill=1.0,
                               base=0, pattern=[[-1, P]], channel_multiplier=1).then_inc(identity_ready, 1)
            pool.wait_ge(ids_loaded, 16)
            for s in STEPS:
                if s[0] == "gather":
                    m, f, t = s[1:]
                    if m >= GATHER_RING and f == t == 0:
                        pool.wait_ge(slot_filled, slot_at["E", m - GATHER_RING] + 1)
                    pool.indirect_dma_start(
                        out=gathered[:, m % GATHER_RING, t, f, :], out_offset=None,
                        in_=tables[2 * m + f],
                        in_offset=bass.IndirectOffsetOnAxis(
                            ap=ids_sb[:, t, 2 * m + f:2 * m + f + 1], axis=0),
                    ).then_inc(fields_gathered[m % GATHER_RING], 16)
                elif by_pool(s):
                    c = s[1]
                    pool.wait_ge(w_high_ready, split_at[s] + 1)
                    low_part(nc.gpsimd, c).then_inc(w_low_pool, 1)

        @block.scalar
        def _(act):
            act.wait_ge(dense_cleared, 1)
            act.dma_start(dense_sb[:, :, 16:32], dense_ctx.rearrange("(t p) d -> p t d", p=P)
                          ).then_inc(small_loaded, 16)
            act.dma_start(b1_sb[:], b_top1.rearrange("(t p) -> p t", p=P),
                          allow_slow_non_contiguous=True).then_inc(small_loaded, 16)
            act.dma_start(b2_sb[:], b_top2.rearrange("(t p) -> p t", p=P),
                          allow_slow_non_contiguous=True).then_inc(small_loaded, 16)
            act.dma_start(w3_sb[:], W_top3.rearrange("(t p) o -> p (t o)", p=P),
                          allow_slow_non_contiguous=True).then_inc(small_loaded, 16)

            for s in STEPS:
                if s[0] == "parts":
                    m = s[1]
                    act.wait_ge(fields_gathered[m % GATHER_RING], 16 * 2 * BT * (m // GATHER_RING + 1))
                    if m >= 2:
                        act.wait_ge(slot_filled, slot_at["E", m - 2])
                    nc.scalar.activation(
                        parts[:, m % 2, :, :, 0, :].bitcast(F32R).rearrange("p t f k -> p (t f) k"),
                        gathered[:, m % GATHER_RING, :, :, :].rearrange("p t f k -> p (t f) k"),
                        ACT.Copy).then_inc(parts_high, 1)
                elif s[0] == "transposes":
                    m = s[1]
                    for f in range(min(2, FIELDS - 1 - 2 * m)):
                        n = slot_at["T", m, f]
                        act.wait_ge(slot_filled, n + 1)
                        nc.scalar.activation(e_parts[:, 2 * m + f, :], slots[:, n % SLOTS, :],
                                             ACT.Copy).then_inc(slot_copied, 1)
                    n = slot_at["E", m]
                    act.wait_ge(slot_filled, n + 1)
                    nc.scalar.activation(e_pairs[:, m, :], slots[:, n % SLOTS, :],
                                         ACT.Copy).then_inc(slot_copied, 1)
                elif s[0] == "weights":
                    c, (m, at) = s[1], chunks[s[1]]
                    act.wait_ge(raw_loaded[m // 2 % 2][at], 16 * loads_of(m // 2, at))
                    if c >= SPLIT_RING:
                        pm, pc = chunks[c - SPLIT_RING]
                        act.wait_ge(slot_filled, slot_at[pm, min(4 * pc + 3, 2 * pm - 1)] + 1)
                    src, rows = raw_chunk(m, at)
                    nc.scalar.activation(
                        w_high[:, c % SPLIT_RING, 0:rows, :].rearrange("p i (j l) -> p i j l", j=2), src,
                        ACT.Copy).then_inc(w_high_ready, 1)
                elif s[0] == "diagonals":
                    g = s[1]
                    act.wait_ge(raw_loaded[g % 2][g], 16 * loads_of(g, g))
                    if g >= 2:
                        act.wait_ge(slot_filled, slot_at["D", 2 * g - 3] + 1)
                    src = raw_diagonals(g).unsqueeze(2).broadcast_to((P, 2, 2, EMBED))
                    nc.scalar.activation(d_high[:, g % 2, :, :, :], src, ACT.Copy).then_inc(w_high_ready, 1)

            act.wait_ge(products_summed, BLOCKS)
            wait_group_split(act, GS - 2)
            for t in (0, 2):
                nc.scalar.activation(z_sb[:, t, :], z_ps[:, t, :], ACT.Copy).then_inc(z_copied[0], 1)
            act.wait_ge(small_loaded, 64)
            for t in (0, 2):
                act.wait_ge(h1_filled, t + 1)
                nc.scalar.activation(h1_sb[:, t, :], slots[:, t, :], ACT.Relu,
                                     bias=b1_sb[:, t:t + 1]).then_inc(h1_ready[0], 1)
            act.wait_ge(h2_filled, 1)
            nc.scalar.activation(h2_sb[:, 0, :], z_ps[:, 0, :], ACT.Relu,
                                 bias=b2_sb[:, 0:1]).then_inc(h2_ready[0], 1)
            act.wait_ge(y_filled, 1)
            nc.scalar.activation(y_sb, z_ps[0:1, 2, :], ACT.Copy).then_inc(y_ready, 1)

        @block.vector
        def _(dve):
            nc.vector.memset(dense_sb[:], 0.0).then_inc(dense_cleared, 1)
            nc.vector.memset(selector[:], 0.0).then_inc(constants_ready, 1)
            nc.vector.memset(zero_row[:], 0.0).then_inc(constants_ready, 1)
            nc.vector.memset(identity[:], 0.0).then_inc(constants_ready, 1)
            dve.wait_ge(constants_ready, 3)
            nc.vector.memset(selector[0:64, 31:32], 1.0).then_inc(constants_ready, 1)
            nc.vector.memset(selector[64:128, 32:33], 1.0).then_inc(constants_ready, 1)

            for s in STEPS:
                if s[0] == "parts":
                    m = s[1]
                    dve.wait_ge(parts_high, m + 1)
                    nc.vector.tensor_tensor(
                        parts[:, m % 2, :, :, 1, :].rearrange("p t f k -> p (t f) k"),
                        gathered[:, m % GATHER_RING, :, :, :].rearrange("p t f k -> p (t f) k"),
                        parts[:, m % 2, :, :, 0, :].rearrange("p t f k -> p (t f) k"),
                        ALU.subtract).then_inc(parts_ready, 1)
                elif s[0] == "weights" and not by_pool(s):
                    dve.wait_ge(w_high_ready, split_at[s] + 1)
                    low_part(nc.vector, s[1]).then_inc(w_low_vector, 1)
                elif s[0] == "diagonals":
                    g = s[1]
                    dve.wait_ge(w_high_ready, split_at[s] + 1)
                    src = raw_diagonals(g).unsqueeze(2).broadcast_to((P, 2, 2, EMBED))
                    nc.vector.tensor_tensor(d_low[:, g % 2, :, :, :], src,
                                            d_high[:, g % 2, :, :, :].bitcast(F32),
                                            ALU.subtract).then_inc(w_low_vector, 1)
                elif s[0] == "diagonal":
                    m = s[1]
                    n = slot_at["D", m]
                    dve.wait_ge(slot_copied, copies_before(slot_at["E", m] + 1))
                    if m % 2 == 0 and m:
                        dve.wait_ge(diagonals_summed, m // 2)
                    dve.wait_ge(slot_filled, n + 1)
                    half = 64 * (m % 2)
                    nc.vector.tensor_tensor(
                        d_products[half:half + 64, :], slots[64:128, n % SLOTS, :], e_pairs[64:128, m, :],
                        ALU.mult).then_inc(diagonals_ready, 1)
                elif s[0] == "block":
                    m, i = s[1:]
                    n, q = slot_at[m, i], product_at[m, i]
                    if q >= PRODUCT_RING:
                        dve.wait_ge(products_summed, q - PRODUCT_RING + 1)
                    dve.wait_ge(slot_filled, n + 1)
                    nc.vector.tensor_tensor(
                        products[:, q % PRODUCT_RING, :], slots[:, n % SLOTS, :], e_pairs[:, m, :],
                        ALU.mult).then_inc(products_ready, 1)

            dve.wait_ge(products_summed, BLOCKS)
            for t in (1, 3):
                nc.vector.tensor_copy(z_sb[:, t, :], z_ps[:, t, :]).then_inc(z_copied[1], 1)
            dve.wait_ge(small_loaded, 64)
            for t in (1, 3):
                dve.wait_ge(h1_filled, t + 1)
                nc.vector.tensor_scalar(h1_sb[:, t, :], slots[:, t, :], b1_sb[:, t:t + 1], 0.0,
                                        ALU.add, ALU.max).then_inc(h1_ready[1], 1)
            dve.wait_ge(h2_filled, 2)
            nc.vector.tensor_scalar(h2_sb[:, 1, :], z_ps[:, 1, :], b2_sb[:, 1:2], 0.0,
                                    ALU.add, ALU.max).then_inc(h2_ready[1], 1)

        @block.tensor
        def _(pe):
            pe.wait_ge(constants_ready, 5)
            for t in range(4):
                for q in range(4):
                    nc.tensor.matmul(z_ps[32 * q:32 * q + 32, t, :], zero_row[:, 0:32], zero_row[:],
                                     start=True, stop=False, skip_group_check=True)
            pe.wait_ge(identity_ready, 1)
            pe.wait_ge(small_loaded, 64)
            for t in range(BT):
                nc.tensor.matmul(z_ps[96:128, 3, P * t:P * t + P], dense_sb[:, t, :], identity[:],
                                 start=False, stop=False, skip_group_check=True)

            def free_slot(n):
                if n >= SLOTS:
                    before = by_slot[n - SLOTS]
                    if before[0] in ("T", "E"):
                        pe.wait_ge(slot_copied, copies_before(n - SLOTS + 1))
                    elif before[0] == "D":
                        pe.wait_ge(diagonals_ready, before[1] + 1)
                    else:
                        pe.wait_ge(products_ready, product_at[before] + 1)

            def sum_blocks(first, count):
                pe.wait_ge(products_ready, first + count)
                for q in range(first, first + count):
                    m, i = block_of[q]
                    lane, quadrant = lane_of(i, m), i % 4
                    t, r = lane // 32, lane % 32
                    last = nc.tensor.matmul(z_ps[32 * quadrant:32 * quadrant + 32, t, :],
                                            selector[:, 31 - r:63 - r], products[:, q % PRODUCT_RING, :],
                                            start=False, stop=m == MS - 1, skip_group_check=True)
                last.then_inc(products_summed, count)

            def sum_diagonals(g):
                pe.wait_ge(diagonals_ready, 2 * g + 2)
                r = DENSE + 2 * g
                nc.tensor.matmul(z_ps[64:96, 3, :], selector[:, 31 - r:63 - r], d_products[:], start=False,
                                 stop=g == GS - 1, skip_group_check=True).then_inc(diagonals_summed, 1)

            summed = d_summed = 0
            for s in STEPS:
                if s[0] == "transposes":
                    m = s[1]
                    pe.wait_ge(parts_ready, m + 1)
                    for f in range(min(2, FIELDS - 1 - 2 * m)):
                        n = slot_at["T", m, f]
                        free_slot(n)
                        for t in range(BT):
                            last = nc.tensor.transpose(
                                slots[:, n % SLOTS, P * t:P * t + P],
                                parts[:, m % 2, t, f, :, :].rearrange("p h k -> p (h k)"), identity[:])
                        last.then_inc(slot_filled, 1)
                    n = slot_at["E", m]
                    free_slot(n)
                    for t in range(BT):
                        last = nc.tensor.transpose(
                            slots[:, n % SLOTS, P * t:P * t + P],
                            gathered[:, m % GATHER_RING, t, :, :].rearrange("p f k -> p (f k)"), identity[:])
                    last.then_inc(slot_filled, 1)
                elif s[0] == "diagonal":
                    m = s[1]
                    n = slot_at["D", m]
                    if m % 2 == 0 and d_summed < m // 2:
                        sum_diagonals(d_summed)
                        d_summed += 1
                    pe.wait_ge(slot_copied, copies_before(slot_at["T", m, 0] + 1))
                    wait_split(pe, "diagonals", m // 2)
                    free_slot(n)
                    for part, weights in enumerate((d_high, d_low)):
                        last = nc.tensor.matmul(
                            slots[:, n % SLOTS, :],
                            weights[:, m // 2 % 2, m % 2, :, :].rearrange("p c l -> p (c l)"),
                            e_parts[:, 2 * m, :], start=part == 0, stop=part == 1)
                    last.then_inc(slot_filled, 1)
                elif s[0] == "block":
                    m, i = s[1:]
                    n, q = slot_at[m, i], product_at[m, i]
                    c = first_chunk(m) + i // 4
                    if i % 4 == 0:
                        wait_split(pe, "weights", c)
                    if i >= 2 * m - 2:
                        pe.wait_ge(slot_copied, copies_before(slot_at["T", i // 2, i % 2] + 1))
                    free_slot(n)
                    for part, weights in enumerate((w_high, w_low)):
                        last = nc.tensor.matmul(slots[:, n % SLOTS, :], weights[:, c % SPLIT_RING, i % 4, :],
                                                e_parts[:, i, :], start=part == 0, stop=part == 1)
                    last.then_inc(slot_filled, 1)
                    if q + 1 - summed >= SUM_LAG + 4:
                        sum_blocks(summed, 4)
                        summed += 4
                        if m % 2 and i >= 6 and d_summed == m // 2:
                            sum_diagonals(d_summed)
                            d_summed += 1
            if d_summed < GS:
                sum_diagonals(d_summed)
            while summed < BLOCKS:
                sum_blocks(summed, 4)
                summed += 4

            pe.wait_ge(w1_loaded, 16 * W1_LOADS)
            pe.wait_ge(z_copied[0], 1)
            for n in range(N1 // P):
                for k in range(4):
                    if n == 0 and k:
                        pe.wait_ge(z_copied[k % 2], k // 2 + 1)
                    last = nc.tensor.matmul(slots[:, n, :], w1_sb[:, k, P * n:P * n + P],
                                            z_sb[:, k, :], start=k == 0, stop=k == 3)
                last.then_inc(h1_filled, 1)
            for n in range(N2 // P):
                for k in range(4):
                    if n == 0:
                        pe.wait_ge(h1_ready[k % 2], k // 2 + 1)
                    last = nc.tensor.matmul(z_ps[:, n, :], w2_sb[:, k, P * n:P * n + P],
                                            h1_sb[:, k, :], start=k == 0, stop=k == 3)
                last.then_inc(h2_filled, 1)
            for k in range(N2 // P):
                pe.wait_ge(h2_ready[k % 2], 1)
                last = nc.tensor.matmul(z_ps[0:1, 2, :], w3_sb[:, k:k + 1], h2_sb[:, k, :],
                                        start=k == 0, stop=k == 1)
            last.then_inc(y_filled, 1)


def kernel(**inputs):
    import numpy as np
    import concourse.bacc as bacc
    from concourse.bass_utils import run_bass_kernel_spmd

    nc = bacc.Bacc("TRN2", target_bir_lowering=False, num_devices=1)
    arrays, aps = {}, {}
    for name, value in inputs.items():
        a = np.ascontiguousarray(value)
        arrays[f"in_{name}"] = a
        aps[name] = nc.dram_tensor(f"in_{name}", a.shape, mybir.dt.from_np(a.dtype),
                                   kind="ExternalInput").ap()
    out = nc.dram_tensor("out_y", (BATCH, 1), F32, kind="ExternalOutput").ap()
    dlrm_tower(nc, aps["dense_ctx"], aps["ids"], [aps[f"tbl_{f}"] for f in range(FIELDS)],
               aps["W_top1"], aps["b_top1"], aps["W_top2"], aps["b_top2"], aps["W_top3"],
               aps["L0_rec_w"], out)
    r = run_bass_kernel_spmd(nc, [arrays], core_ids=[0])
    return r.results[0]["out_y"]
```

```python
from contextlib import ExitStack

import concourse.bass as bass
from concourse import mybir

F32 = mybir.dt.float32
F32R = mybir.dt.float32r
BF16 = mybir.dt.bfloat16
I32 = mybir.dt.int32
ALU = mybir.AluOpType
ACT = mybir.ActivationFunctionType

P = 128
FIELDS = 32
EMBED = 64
BATCH = 512
BT = BATCH // P
MS = FIELDS // 2
GS = FIELDS // 4
DENSE = 16
N1, N2 = 512, 256
SPLIT_RING = 3
SLOTS = 4
PRODUCT_RING = 8
GATHER_RING = 4
POOL_SPLITS_FROM = 8
SUM_LAG = 4
GATHER = 1.0
POOL_SPLIT = 1.2
BLOCK = 0.65
DIAGONAL = 0.65
TRANSPOSES = 0.4
LANDING = 2.0
BLOCKS_LEFT = 4
LOWS_AFTER = 2
SPLIT_AHEAD = 2


def pair(i, j):
    return i * (FIELDS - 1) - i * (i - 1) // 2 + j - i - 1


def lane_of(i, m):
    before = sum(2 * (MS - 1 - a // 2) for a in range(i % 4, i, 4))
    return before + 2 * (m - i // 2 - 1)


def chunks_of(m):
    return (2 * m + 3) // 4


def first_chunk(m):
    return sum(chunks_of(a) for a in range(m))


def chunk_list():
    return [(m, c) for m in range(MS) for c in range(chunks_of(m))]


def schedule():
    chunks = chunk_list()
    gathers = [(m, t, f) for m in range(MS) for t in range(BT) for f in range(2)]
    steps, landed, taken_at = [], {}, {}
    pool = tensor = 0.0
    gathered = split = taken = 0
    lows_due = None

    def gather_until(limit):
        nonlocal pool, gathered
        while gathered < len(gathers) and gathers[gathered][0] < taken + GATHER_RING and pool < limit:
            steps.append(("gather", *gathers[gathered]))
            if gathers[gathered][0] >= GATHER_RING:
                pool = max(pool, taken_at[gathers[gathered][0] - GATHER_RING])
            pool += GATHER
            landed[gathers[gathered][0]] = pool + LANDING
            gathered += 1

    def split_chunk():
        nonlocal pool, split
        if split < len(chunks):
            if chunks[split][0] >= POOL_SPLITS_FROM:
                gather_until(tensor)
                pool = max(pool, tensor) + POOL_SPLIT
            steps.append(("weights", split))
            split += 1

    def take_fields():
        nonlocal tensor, taken, lows_due
        gather_until(float("inf") if gathered < 8 * (taken + 1) else tensor)
        tensor = max(tensor, landed[taken])
        steps.append(("fields", taken))
        tensor += TRANSPOSES
        taken_at[taken] = tensor
        taken += 1
        lows_due = LOWS_AFTER

    def make_lows():
        nonlocal lows_due
        if lows_due is not None:
            steps.append(("lows", taken - 1))
            lows_due = None

    steps.append(("diagonals", 0))
    for _ in range(SPLIT_AHEAD):
        split_chunk()
    for m in range(MS):
        if taken == m:
            take_fields()
        if taken == m + 1:
            make_lows()
        gather_until(tensor)
        steps.append(("diagonal", m))
        tensor += DIAGONAL
        if m % 2 and m // 2 + 1 < GS:
            steps.append(("diagonals", m // 2 + 1))
        for i in range(2 * m):
            steps.append(("block", m, i))
            tensor += BLOCK
            if lows_due is not None:
                lows_due -= 1
                if lows_due <= 0:
                    make_lows()
            if i % 4 == 0:
                split_chunk()
            gather_until(tensor)
            if lows_due is None and taken < MS and (
                    taken == m + 1 and i >= 2 * m - 1 - BLOCKS_LEFT
                    or gathered >= 8 * (taken + 1) and tensor >= landed[taken]):
                take_fields()
    make_lows()
    assert taken == MS and gathered == len(gathers) and split == len(chunks)
    return steps


def sum_batches():
    return [[(m, i) for i in range(c, min(c + 4, 2 * m))] for m in range(MS) for c in range(0, 2 * m, 4)]


def dlrm_tower(nc, dense_ctx, ids, tables, W_top1, b_top1, W_top2, b_top2, W_top3, w, out):
    STEPS = schedule()
    slot_at = {}
    product_at = {}
    split_at = {}
    for s in STEPS:
        if s[0] == "fields":
            slot_at["E", s[1]] = len(slot_at)
        elif s[0] == "diagonal":
            slot_at["D", s[1]] = len(slot_at)
        elif s[0] == "block":
            slot_at[s[1:]] = len(slot_at)
            product_at[s[1:]] = len(product_at)
        elif s[0] in ("weights", "diagonals"):
            split_at[s] = len(split_at)
    by_slot = {n: k for k, n in slot_at.items()}
    BLOCKS = len(product_at)
    chunks = chunk_list()
    def loads_of(g, c):
        return sum(5 if c < a else 6 for a in range(g % 2, g + 1, 2) if c <= a)

    def by_pool(step):
        return step[0] == "weights" and chunks[step[1]][0] >= POOL_SPLITS_FROM

    low_at = {}
    for s in STEPS:
        if s in split_at:
            low_at[s] = sum(by_pool(a) == by_pool(s) for a in low_at)

    with ExitStack() as ctx:
        def sb(name, shape, dt=F32):
            return ctx.enter_context(nc.sbuf_tensor(name, shape, dt))

        def sem(name):
            return ctx.enter_context(nc.semaphore(name))

        ids_sb = sb("ids_sb", [P, BT, FIELDS], I32)
        gathered = sb("gathered", [P, GATHER_RING, BT, 2, EMBED])
        e_parts = sb("e_parts", [P, FIELDS, BATCH], F32R)
        e_pairs = sb("e_pairs", [P, MS, BATCH])
        raw_rows = [4 * (GS - 1), 4 * GS]
        raw = [sb(f"raw{h}", [P, raw_rows[h], 4, EMBED]) for h in range(2)]
        w_high = sb("w_high", [P, SPLIT_RING, 4, 2 * EMBED], F32R)
        w_low = sb("w_low", [P, SPLIT_RING, 4, 2 * EMBED], F32R)
        d_high = sb("d_high", [P, 2, 2, 2, EMBED], F32R)
        d_low = sb("d_low", [P, 2, 2, 2, EMBED], F32R)
        products = sb("products", [P, PRODUCT_RING, BATCH])
        d_products = sb("d_products", [P, 2, BATCH])
        selector = sb("selector", [P, 2 * 32])
        identity = sb("identity", [P, P])
        zero_row = sb("zero_row", [1, BATCH], BF16)
        dense_sb = sb("dense_sb", [P, BT, 32])
        b1_sb = sb("b1_sb", [P, N1 // P])
        b2_sb = sb("b2_sb", [P, N2 // P])
        w3_sb = sb("w3_sb", [P, N2 // P])

        tail = raw[0][:].rearrange("p i j l -> p (i j l)")
        w1_sb = tail[:, 0:4 * N1].rearrange("p (t n) -> p t n", t=4)
        w2_sb = tail[:, 4 * N1:4 * N1 + 4 * N2].rearrange("p (t n) -> p t n", t=4)
        z_sb = tail[:, 3072:3072 + 4 * BATCH].rearrange("p (t b) -> p t b", t=4)
        h1_sb = tail[:, 5120:5120 + 4 * BATCH].rearrange("p (t b) -> p t b", t=4)
        h2_sb = e_pairs[:, 0:2, :]
        y_sb = e_pairs[0:1, 2, :]

        z_ps = ctx.enter_context(nc.psum_tensor("z_ps", [P, 4, BATCH], F32))
        slots = ctx.enter_context(nc.psum_tensor("slots", [P, SLOTS, BATCH], F32))

        ids_loaded = sem("ids_loaded")
        small_loaded = sem("small_loaded")
        w1_loaded = sem("w1_loaded")
        raw_loaded = [[sem(f"raw{h}_rows{4 * c}_loaded") for c in range(GS)] for h in range(2)]
        fields_gathered = [[sem(f"fields_gathered{h}_tile{t}") for t in range(BT)]
                           for h in range(GATHER_RING)]
        constants_ready = sem("constants_ready")
        identity_ready = sem("identity_ready")
        dense_cleared = sem("dense_cleared")
        fields_copied = sem("fields_copied")
        fields_low = sem("fields_low")
        w_high_ready = sem("w_high_ready")
        w_low_vector = sem("w_low_vector")
        w_low_pool = sem("w_low_pool")
        slot_filled = sem("slot_filled")
        products_ready = sem("products_ready")
        diagonals_ready = sem("diagonals_ready")
        diagonals_summed = sem("diagonals_summed")
        products_summed = sem("products_summed")
        z_copied = [sem("z_copied_act"), sem("z_copied_dve")]
        h1_filled = sem("h1_filled")
        h1_ready = [sem("h1_ready_act"), sem("h1_ready_dve")]
        h2_filled = sem("h2_filled")
        h2_ready = [sem("h2_ready_act"), sem("h2_ready_dve")]
        y_filled = sem("y_filled")
        y_ready = sem("y_ready")
        y_stored = sem("y_stored")

        def wait_split(engine, *step):
            engine.wait_ge(w_low_pool if by_pool(step) else w_low_vector, low_at[step] + 1)

        def wait_rows_split(engine, g, c):
            if c < chunks_of(2 * g + 1):
                wait_split(engine, "weights", first_chunk(2 * g + 1) + c)
            if c == g:
                wait_split(engine, "diagonals", g)

        def wait_group_split(engine, g):
            wait_rows_split(engine, g, g)

        def raw_chunk(m, c):
            g = m // 2
            rows = min(4, 2 * m - 4 * c)
            j = 2 * (m % 2)
            return raw[g % 2][:, 4 * c:4 * c + rows, j:j + 2, :], rows

        def raw_diagonals(g):
            flat = raw[g % 2][:].rearrange("p i j l -> p (i j) l")
            return flat[:, 16 * g + 1:16 * g + 12:10, :]

        W1_LOADS = 2 + MS + sum(
            1 + (lane_of(i, MS - 1) + 1) // 32 - lane_of(i, i // 2 + 1) // 32 for i in range(FIELDS - 2))

        def low_part(engine, c):
            src, rows = raw_chunk(*chunks[c])
            low, high = (x[:, c % SPLIT_RING, 0:rows, :].rearrange("p i (j l) -> p i j l", j=2)
                         for x in (w_low, w_high[:].bitcast(F32)))
            return engine.tensor_tensor(low, src, high, ALU.subtract)

        block = ctx.enter_context(nc.Block())

        @block.sync
        def _(sp):
            sp.dma_start(ids_sb[:], ids.rearrange("(t p) f -> p t f", p=P)).then_inc(ids_loaded, 16)

            def load_raw(g, c):
                for i in range(4 * c, min(4 * c + 4, 4 * g + 3)):
                    j = max(4 * g, i + 1)
                    k = 4 * g + 4 - j
                    src = w[pair(i, j):pair(i, j) + k, :, :].rearrange("p k l -> k p l")
                    for half in range(1 if c < g else 2):
                        sp.dma_start(raw[g % 2][64 * half:64 * half + 64, i, 4 - k:4, :], src
                                     ).then_inc(raw_loaded[g % 2][c], 16)

            def copy_raw(g, c):
                if c < g:
                    sp.wait_ge(raw_loaded[g % 2][c], 16 * (loads_of(g, c) - 1))
                    sp.dma_start(raw[g % 2][64:128, 4 * c:4 * c + 4, :, :],
                                 raw[g % 2][0:64, 4 * c:4 * c + 4, :, :]).then_inc(raw_loaded[g % 2][c], 16)

            before = None
            for g in range(GS):
                for c in range(g + 1):
                    if g >= 2 and c < g - 1:
                        wait_rows_split(sp, g - 2, c)
                    load_raw(g, c)
                    if before:
                        copy_raw(*before)
                    before = g, c

            wait_group_split(sp, GS - 2)
            sp.dma_start(w2_sb, W_top2.rearrange("(t p) n -> p t n", p=P)).then_inc(w1_loaded, 16)
            n = 1
            for i in range(FIELDS - 2):
                lane, row, left = lane_of(i, i // 2 + 1), pair(i, 2 * (i // 2 + 1)), 2 * (MS - 1 - i // 2)
                while left:
                    t, r = lane // 32, lane % 32
                    k = min(left, 32 - r)
                    at = 32 * (i % 4) + r
                    sp.dma_start(w1_sb[at:at + k, t, :], W_top1[row:row + k, :]).then_inc(w1_loaded, 16)
                    lane, row, left, n = lane + k, row + k, left - k, n + 1
            for m in range(MS):
                row = pair(2 * m, 2 * m + 1)
                sp.dma_start(w1_sb[80 + m:81 + m, 3, :], W_top1[row:row + 1, :]).then_inc(w1_loaded, 16)
            sp.dma_start(w1_sb[112:128, 3, :], W_top1[N1 - DENSE:N1, :]).then_inc(w1_loaded, 16)
            assert n + MS + 1 == W1_LOADS
            sp.wait_ge(y_ready, 1)
            sp.dma_start(out.rearrange("b o -> o b"), y_sb).then_inc(y_stored, 16)
            sp.wait_ge(y_stored, 16)

        @block.gpsimd
        def _(pool):
            pool.wait_ge(constants_ready, 3)
            pool.affine_select(out=identity[:], in_=identity[:], compare_op=ALU.not_equal, fill=1.0,
                               base=0, pattern=[[-1, P]], channel_multiplier=1).then_inc(identity_ready, 1)
            pool.wait_ge(ids_loaded, 16)
            for s in STEPS:
                if s[0] == "gather":
                    m, t, f = s[1:]
                    if m >= GATHER_RING and f == t == 0:
                        pool.wait_ge(slot_filled, slot_at["E", m - GATHER_RING] + 1)
                    pool.indirect_dma_start(
                        out=gathered[:, m % GATHER_RING, t, f, :], out_offset=None,
                        in_=tables[2 * m + f],
                        in_offset=bass.IndirectOffsetOnAxis(
                            ap=ids_sb[:, t, 2 * m + f:2 * m + f + 1], axis=0),
                    ).then_inc(fields_gathered[m % GATHER_RING][t], 16)
                elif by_pool(s):
                    c = s[1]
                    pool.wait_ge(w_high_ready, split_at[s] + 1)
                    low_part(nc.gpsimd, c).then_inc(w_low_pool, 1)

        @block.scalar
        def _(act):
            act.wait_ge(dense_cleared, 1)
            act.dma_start(dense_sb[:, :, 16:32], dense_ctx.rearrange("(t p) d -> p t d", p=P)
                          ).then_inc(small_loaded, 16)
            act.dma_start(b1_sb[:], b_top1.rearrange("(t p) -> p t", p=P),
                          allow_slow_non_contiguous=True).then_inc(small_loaded, 16)
            act.dma_start(b2_sb[:], b_top2.rearrange("(t p) -> p t", p=P),
                          allow_slow_non_contiguous=True).then_inc(small_loaded, 16)
            act.dma_start(w3_sb[:], W_top3.rearrange("(t p) o -> p (t o)", p=P),
                          allow_slow_non_contiguous=True).then_inc(small_loaded, 16)

            for s in STEPS:
                if s[0] == "fields":
                    m = s[1]
                    n = slot_at["E", m]
                    act.wait_ge(slot_filled, n + 1)
                    nc.scalar.activation(e_pairs[:, m, :], slots[:, n % SLOTS, :], ACT.Copy)
                    nc.scalar.activation(e_parts[0:64, 2 * m, :], slots[0:64, n % SLOTS, :], ACT.Copy)
                    nc.scalar.activation(e_parts[64:128, 2 * m + 1, :], slots[64:128, n % SLOTS, :],
                                         ACT.Copy).then_inc(fields_copied, 1)
                elif s[0] == "weights":
                    c, (m, at) = s[1], chunks[s[1]]
                    act.wait_ge(raw_loaded[m // 2 % 2][at], 16 * loads_of(m // 2, at))
                    if c >= SPLIT_RING:
                        pm, pc = chunks[c - SPLIT_RING]
                        act.wait_ge(slot_filled, slot_at[pm, min(4 * pc + 3, 2 * pm - 1)] + 1)
                    src, rows = raw_chunk(m, at)
                    nc.scalar.activation(
                        w_high[:, c % SPLIT_RING, 0:rows, :].rearrange("p i (j l) -> p i j l", j=2), src,
                        ACT.Copy).then_inc(w_high_ready, 1)
                elif s[0] == "diagonals":
                    g = s[1]
                    act.wait_ge(raw_loaded[g % 2][g], 16 * loads_of(g, g))
                    if g >= 2:
                        act.wait_ge(slot_filled, slot_at["D", 2 * g - 3] + 1)
                    src = raw_diagonals(g).unsqueeze(2).broadcast_to((P, 2, 2, EMBED))
                    nc.scalar.activation(d_high[:, g % 2, :, :, :], src, ACT.Copy).then_inc(w_high_ready, 1)

            act.wait_ge(products_summed, BLOCKS)
            wait_group_split(act, GS - 2)
            for t in (0, 2):
                nc.scalar.activation(z_sb[:, t, :], z_ps[:, t, :], ACT.Copy).then_inc(z_copied[0], 1)
            act.wait_ge(small_loaded, 64)
            for t in (0, 2):
                act.wait_ge(h1_filled, t + 1)
                nc.scalar.activation(h1_sb[:, t, :], slots[:, t, :], ACT.Relu,
                                     bias=b1_sb[:, t:t + 1]).then_inc(h1_ready[0], 1)
            act.wait_ge(h2_filled, 1)
            nc.scalar.activation(h2_sb[:, 0, :], z_ps[:, 0, :], ACT.Relu,
                                 bias=b2_sb[:, 0:1]).then_inc(h2_ready[0], 1)
            act.wait_ge(y_filled, 1)
            nc.scalar.activation(y_sb, z_ps[0:1, 2, :], ACT.Copy).then_inc(y_ready, 1)

        @block.vector
        def _(dve):
            nc.vector.memset(dense_sb[:], 0.0).then_inc(dense_cleared, 1)
            nc.vector.memset(selector[:], 0.0).then_inc(constants_ready, 1)
            nc.vector.memset(zero_row[:], 0.0).then_inc(constants_ready, 1)
            nc.vector.memset(identity[:], 0.0).then_inc(constants_ready, 1)
            dve.wait_ge(constants_ready, 3)
            nc.vector.memset(selector[0:64, 31:32], 1.0).then_inc(constants_ready, 1)
            nc.vector.memset(selector[64:128, 32:33], 1.0).then_inc(constants_ready, 1)

            for s in STEPS:
                if s[0] == "lows":
                    m = s[1]
                    dve.wait_ge(fields_copied, m + 1)
                    nc.vector.tensor_tensor(
                        e_parts[64:128, 2 * m, :], e_pairs[0:64, m, :],
                        e_parts[0:64, 2 * m, :].bitcast(F32), ALU.subtract)
                    nc.vector.tensor_tensor(
                        e_parts[0:64, 2 * m + 1, :], e_pairs[64:128, m, :],
                        e_parts[64:128, 2 * m + 1, :].bitcast(F32), ALU.subtract).then_inc(fields_low, 1)
                elif s[0] == "weights" and not by_pool(s):
                    dve.wait_ge(w_high_ready, split_at[s] + 1)
                    low_part(nc.vector, s[1]).then_inc(w_low_vector, 1)
                elif s[0] == "diagonals":
                    g = s[1]
                    dve.wait_ge(w_high_ready, split_at[s] + 1)
                    src = raw_diagonals(g).unsqueeze(2).broadcast_to((P, 2, 2, EMBED))
                    nc.vector.tensor_tensor(d_low[:, g % 2, :, :, :], src,
                                            d_high[:, g % 2, :, :, :].bitcast(F32),
                                            ALU.subtract).then_inc(w_low_vector, 1)
                elif s[0] == "diagonal":
                    m = s[1]
                    n = slot_at["D", m]
                    if m % 2 == 0 and m >= 4:
                        dve.wait_ge(diagonals_summed, m // 2 - 1)
                    dve.wait_ge(slot_filled, n + 1)
                    half = 64 * (m % 2)
                    nc.vector.tensor_tensor(
                        d_products[half:half + 64, m // 2 % 2, :], slots[64:128, n % SLOTS, :], e_pairs[64:128, m, :],
                        ALU.mult).then_inc(diagonals_ready, 1)
                elif s[0] == "block":
                    m, i = s[1:]
                    n, q = slot_at[m, i], product_at[m, i]
                    if q >= PRODUCT_RING:
                        dve.wait_ge(products_summed, q - PRODUCT_RING + 1)
                    dve.wait_ge(slot_filled, n + 1)
                    nc.vector.tensor_tensor(
                        products[:, q % PRODUCT_RING, :], slots[:, n % SLOTS, :], e_pairs[:, m, :],
                        ALU.mult).then_inc(products_ready, 1)

            dve.wait_ge(products_summed, BLOCKS)
            dve.wait_ge(diagonals_summed, GS)
            for t in (1, 3):
                nc.vector.tensor_copy(z_sb[:, t, :], z_ps[:, t, :]).then_inc(z_copied[1], 1)
            dve.wait_ge(small_loaded, 64)
            for t in (1, 3):
                dve.wait_ge(h1_filled, t + 1)
                nc.vector.tensor_scalar(h1_sb[:, t, :], slots[:, t, :], b1_sb[:, t:t + 1], 0.0,
                                        ALU.add, ALU.max).then_inc(h1_ready[1], 1)
            dve.wait_ge(h2_filled, 2)
            nc.vector.tensor_scalar(h2_sb[:, 1, :], z_ps[:, 1, :], b2_sb[:, 1:2], 0.0,
                                    ALU.add, ALU.max).then_inc(h2_ready[1], 1)

        @block.tensor
        def _(pe):
            pe.wait_ge(constants_ready, 5)
            for t in range(4):
                for q in range(4):
                    nc.tensor.matmul(z_ps[32 * q:32 * q + 32, t, :], zero_row[:, 0:32], zero_row[:],
                                     start=True, stop=False, skip_group_check=True)
            pe.wait_ge(identity_ready, 1)
            pe.wait_ge(small_loaded, 64)
            for t in range(BT):
                nc.tensor.matmul(z_ps[96:128, 3, P * t:P * t + P], dense_sb[:, t, :], identity[:],
                                 start=False, stop=False, skip_group_check=True)

            def free_slot(n):
                if n >= SLOTS:
                    before = by_slot[n - SLOTS]
                    if before[0] == "E":
                        pe.wait_ge(fields_copied, before[1] + 1)
                    elif before[0] == "D":
                        pe.wait_ge(diagonals_ready, before[1] + 1)
                    else:
                        pe.wait_ge(products_ready, product_at[before] + 1)

            def sum_over_l(quadrant, lane, of, last):
                t, r = lane // 32, lane % 32
                return nc.tensor.matmul(z_ps[32 * quadrant:32 * quadrant + 32, t, :],
                                        selector[:, 31 - r:63 - r], of, start=False, stop=last,
                                        skip_group_check=True)

            def sum_batch(batch):
                m = batch[0][0]
                pe.wait_ge(products_ready, product_at[batch[-1]] + 1)
                for _, i in batch:
                    summed = sum_over_l(i % 4, lane_of(i, m), products[:, product_at[m, i] % PRODUCT_RING, :],
                                        m == MS - 1)
                summed.then_inc(products_summed, len(batch))
                if m % 2 and batch[-1][1] == 2 * m - 1:
                    g = m // 2
                    pe.wait_ge(diagonals_ready, 2 * g + 2)
                    sum_over_l(2, 96 + DENSE + 2 * g, d_products[:, g % 2, :], g == GS - 1
                               ).then_inc(diagonals_summed, 1)

            unsummed = sum_batches()
            for s in STEPS:
                if s[0] == "fields":
                    m = s[1]
                    n = slot_at["E", m]
                    free_slot(n)
                    for t in range(BT):
                        pe.wait_ge(fields_gathered[m % GATHER_RING][t], 16 * 2 * (m // GATHER_RING + 1))
                        last = nc.tensor.transpose(
                            slots[:, n % SLOTS, P * t:P * t + P],
                            gathered[:, m % GATHER_RING, t, :, :].rearrange("p f k -> p (f k)"), identity[:])
                    last.then_inc(slot_filled, 1)
                elif s[0] == "diagonal":
                    m = s[1]
                    n = slot_at["D", m]
                    pe.wait_ge(fields_low, m + 1)
                    wait_split(pe, "diagonals", m // 2)
                    free_slot(n)
                    for part, weights in enumerate((d_high, d_low)):
                        last = nc.tensor.matmul(
                            slots[:, n % SLOTS, :],
                            weights[:, m // 2 % 2, m % 2, :, :].rearrange("p c l -> p (c l)"),
                            e_parts[:, 2 * m, :], start=part == 0, stop=part == 1)
                    last.then_inc(slot_filled, 1)
                elif s[0] == "block":
                    m, i = s[1:]
                    n, q = slot_at[m, i], product_at[m, i]
                    c = first_chunk(m) + i // 4
                    if i % 4 == 0:
                        wait_split(pe, "weights", c)
                    free_slot(n)
                    for part, weights in enumerate((w_high, w_low)):
                        last = nc.tensor.matmul(slots[:, n % SLOTS, :], weights[:, c % SPLIT_RING, i % 4, :],
                                                e_parts[:, i, :], start=part == 0, stop=part == 1)
                    last.then_inc(slot_filled, 1)
                    if q >= product_at[unsummed[0][-1]] + SUM_LAG:
                        sum_batch(unsummed.pop(0))
            for batch in unsummed:
                sum_batch(batch)

            pe.wait_ge(w1_loaded, 16 * W1_LOADS)
            pe.wait_ge(z_copied[0], 1)
            for n in range(N1 // P):
                for k in range(4):
                    if n == 0 and k:
                        pe.wait_ge(z_copied[k % 2], k // 2 + 1)
                    last = nc.tensor.matmul(slots[:, n, :], w1_sb[:, k, P * n:P * n + P],
                                            z_sb[:, k, :], start=k == 0, stop=k == 3)
                last.then_inc(h1_filled, 1)
            for n in range(N2 // P):
                for k in range(4):
                    if n == 0:
                        pe.wait_ge(h1_ready[k % 2], k // 2 + 1)
                    last = nc.tensor.matmul(z_ps[:, n, :], w2_sb[:, k, P * n:P * n + P],
                                            h1_sb[:, k, :], start=k == 0, stop=k == 3)
                last.then_inc(h2_filled, 1)
            for k in range(N2 // P):
                pe.wait_ge(h2_ready[k % 2], 1)
                last = nc.tensor.matmul(z_ps[0:1, 2, :], w3_sb[:, k:k + 1], h2_sb[:, k, :],
                                        start=k == 0, stop=k == 1)
            last.then_inc(y_filled, 1)


def kernel(**inputs):
    import numpy as np
    import concourse.bacc as bacc
    from concourse.bass_utils import run_bass_kernel_spmd

    nc = bacc.Bacc("TRN2", target_bir_lowering=False, num_devices=1)
    arrays, aps = {}, {}
    for name, value in inputs.items():
        a = np.ascontiguousarray(value)
        arrays[f"in_{name}"] = a
        aps[name] = nc.dram_tensor(f"in_{name}", a.shape, mybir.dt.from_np(a.dtype),
                                   kind="ExternalInput").ap()
    out = nc.dram_tensor("out_y", (BATCH, 1), F32, kind="ExternalOutput").ap()
    dlrm_tower(nc, aps["dense_ctx"], aps["ids"], [aps[f"tbl_{f}"] for f in range(FIELDS)],
               aps["W_top1"], aps["b_top1"], aps["W_top2"], aps["b_top2"], aps["W_top3"],
               aps["L0_rec_w"], out)
    r = run_bass_kernel_spmd(nc, [arrays], core_ids=[0])
    return r.results[0]["out_y"]
```

```python
from contextlib import ExitStack

import concourse.bass as bass
from concourse import mybir

F32 = mybir.dt.float32
F32R = mybir.dt.float32r
BF16 = mybir.dt.bfloat16
I32 = mybir.dt.int32
ALU = mybir.AluOpType
ACT = mybir.ActivationFunctionType

P = 128
FIELDS = 32
EMBED = 64
BATCH = 512
BT = BATCH // P
MS = FIELDS // 2
GS = FIELDS // 4
DENSE = 16
N1, N2 = 512, 256
SPLIT_RING = 4
SLOTS = 4
PRODUCT_RING = 8
GATHER_RING = 4
POOL_SPLITS_FROM = 8
SUM_LAG = 4
POOL_SPLIT = 1.2
BLOCK = 0.66
DIAGONAL = 0.41
TRANSPOSES = 0.45
VECTOR = 0.58
LANDING = 2.5
FIELDS_SPLIT = 4.0
BLOCKS_LEFT = 3
LOWS_AFTER = 1
DIAGONALS_AFTER = 0
SPLIT_AHEAD = 3


def pair(i, j):
    return i * (FIELDS - 1) - i * (i - 1) // 2 + j - i - 1


def lane_of(i, m):
    before = sum(2 * (MS - 1 - a // 2) for a in range(i % 4, i, 4))
    return before + 2 * (m - i // 2 - 1)


def chunks_of(m):
    return (2 * m + 3) // 4


def first_chunk(m):
    return sum(chunks_of(a) for a in range(m))


def chunk_list():
    return [(m, c) for m in range(MS) for c in range(chunks_of(m))]


def schedule():
    chunks = chunk_list()
    gathers = [(m, t, f) for m in range(MS) for t in range(BT) for f in range(2)]
    steps, landed, taken_at = [], {}, {}
    pool = tensor = vector = 0.0
    gathered = split = taken = 0
    lows_due = None

    def gather_until(limit):
        nonlocal pool, gathered
        while gathered < len(gathers) and gathers[gathered][0] < taken + GATHER_RING and pool < limit:
            steps.append(("gather", *gathers[gathered]))
            if gathers[gathered][0] >= GATHER_RING:
                pool = max(pool, taken_at[gathers[gathered][0] - GATHER_RING])
            pool += 1
            landed[gathers[gathered][0]] = pool + LANDING
            gathered += 1

    def vector_step():
        nonlocal tensor, vector
        vector = max(vector, tensor) + VECTOR
        tensor = max(tensor, vector - (SLOTS - 1) * VECTOR)

    def split_chunk():
        nonlocal pool, split
        if split < len(chunks):
            if chunks[split][0] >= POOL_SPLITS_FROM:
                gather_until(tensor)
                pool = max(pool, tensor) + POOL_SPLIT
            else:
                vector_step()
            steps.append(("weights", split))
            split += 1

    def take_fields():
        nonlocal tensor, taken, lows_due
        gather_until(float("inf") if gathered < 8 * (taken + 1) else tensor)
        tensor = max(tensor, landed[taken])
        steps.append(("fields", taken))
        tensor += TRANSPOSES
        taken_at[taken] = tensor
        taken += 1
        lows_due = LOWS_AFTER

    def make_lows():
        nonlocal lows_due
        if lows_due is not None:
            vector_step()
            steps.append(("lows", taken - 1))
            lows_due = None

    steps.append(("diagonals", 0))
    for _ in range(SPLIT_AHEAD):
        split_chunk()
    for m in range(MS):
        if taken == m:
            take_fields()
        if taken == m + 1:
            make_lows()
        tensor = max(tensor, taken_at[m] + FIELDS_SPLIT)
        gather_until(tensor)
        steps.append(("diagonal", m))
        tensor += DIAGONAL
        vector_step()
        for i in range(2 * m):
            steps.append(("block", m, i))
            tensor += BLOCK
            vector_step()
            if m % 2 and i == min(2 * m - 1, DIAGONALS_AFTER) and m // 2 + 1 < GS:
                steps.append(("diagonals", m // 2 + 1))
            if lows_due is not None:
                lows_due -= 1
                if lows_due <= 0:
                    make_lows()
            if i % 4 == 0:
                split_chunk()
            gather_until(tensor)
            if lows_due is None and taken < MS and (
                    taken == m + 1 and i >= 2 * m - 1 - BLOCKS_LEFT
                    or gathered >= 8 * (taken + 1) and tensor >= landed[taken]):
                take_fields()
    make_lows()
    assert taken == MS and gathered == len(gathers) and split == len(chunks)
    return steps


def sum_batches():
    return [[(m, i) for i in range(c, min(c + 4, 2 * m))] for m in range(MS) for c in range(0, 2 * m, 4)]


def dlrm_tower(nc, dense_ctx, ids, tables, W_top1, b_top1, W_top2, b_top2, W_top3, w, out):
    STEPS = schedule()
    slot_at = {}
    product_at = {}
    split_at = {}
    for s in STEPS:
        if s[0] == "fields":
            slot_at["E", s[1]] = len(slot_at)
        elif s[0] == "diagonal":
            slot_at["D", s[1]] = len(slot_at)
        elif s[0] == "block":
            slot_at[s[1:]] = len(slot_at)
            product_at[s[1:]] = len(product_at)
        elif s[0] in ("weights", "diagonals"):
            split_at[s] = len(split_at)
    by_slot = {n: k for k, n in slot_at.items()}
    chunks = chunk_list()

    def loads_of(g, c):
        return sum(5 if c < a else 6 for a in range(g % 2, g + 1, 2) if c <= a)

    def by_pool(step):
        return step[0] == "weights" and chunks[step[1]][0] >= POOL_SPLITS_FROM

    low_at = {}
    for s in STEPS:
        if s in split_at:
            low_at[s] = sum(by_pool(a) == by_pool(s) for a in low_at)

    with ExitStack() as ctx:
        def sb(name, shape, dt=F32):
            return ctx.enter_context(nc.sbuf_tensor(name, shape, dt))

        def sem(name):
            return ctx.enter_context(nc.semaphore(name))

        ids_sb = sb("ids_sb", [P, BT, FIELDS], I32)
        gathered = sb("gathered", [P, GATHER_RING, BT, 2, EMBED])
        e_parts = sb("e_parts", [P, FIELDS - 1, BATCH], F32R)
        pair_part = sb("pair_part", [P, BATCH], F32R)
        e_pairs = sb("e_pairs", [P, MS, BATCH])
        raw_rows = [4 * (GS - 1), 4 * GS]
        raw = [sb(f"raw{h}", [P, raw_rows[h], 4, EMBED]) for h in range(2)]
        w_high = sb("w_high", [P, SPLIT_RING, 4, 2 * EMBED], F32R)
        w_low = sb("w_low", [P, SPLIT_RING, 4, 2 * EMBED], F32R)
        d_high = sb("d_high", [P, 2, 2, 2, EMBED], F32R)
        d_low = sb("d_low", [P, 2, 2, 2, EMBED], F32R)
        products = sb("products", [P, PRODUCT_RING, BATCH])
        d_products = sb("d_products", [P, 2, BATCH])
        selector = sb("selector", [P, 2 * 32])
        identity = sb("identity", [P, P])
        zero_row = products[0:1, PRODUCT_RING - 1, :].bitcast(BF16)[:, 0:BATCH]
        dense_sb = sb("dense_sb", [P, BT, 32])
        b1_sb = sb("b1_sb", [P, N1 // P])
        b2_sb = sb("b2_sb", [P, N2 // P])
        w3_sb = sb("w3_sb", [P, N2 // P])

        tail = raw[0][:].rearrange("p i j l -> p (i j l)")
        w1_sb = tail[:, 0:4 * N1].rearrange("p (t n) -> p t n", t=4)
        w2_sb = tail[:, 4 * N1:4 * N1 + 4 * N2].rearrange("p (t n) -> p t n", t=4)
        z_sb = tail[:, 3072:3072 + 4 * BATCH].rearrange("p (t b) -> p t b", t=4)
        h1_sb = tail[:, 5120:5120 + 4 * BATCH].rearrange("p (t b) -> p t b", t=4)
        h2_sb = e_pairs[:, 0:2, :]
        y_sb = e_pairs[:, 2, 0:P]

        z_ps = ctx.enter_context(nc.psum_tensor("z_ps", [P, 4, BATCH], F32))
        slots = ctx.enter_context(nc.psum_tensor("slots", [P, SLOTS, BATCH], F32))

        ids_loaded = sem("ids_loaded")
        small_loaded = sem("small_loaded")
        w1_loaded = sem("w1_loaded")
        raw_loaded = [[sem(f"raw{h}_rows{4 * c}_loaded") for c in range(GS)] for h in range(2)]
        fields_gathered = [[sem(f"fields_gathered{h}_tile{t}") for t in range(BT)]
                           for h in range(GATHER_RING)]
        constants_ready = sem("constants_ready")
        identity_ready = sem("identity_ready")
        dense_cleared = sem("dense_cleared")
        pair_copied = sem("pair_copied")
        fields_high = sem("fields_high")
        pair_split = sem("pair_split")
        fields_low = sem("fields_low")
        w_high_ready = sem("w_high_ready")
        w_low_vector = sem("w_low_vector")
        w_low_pool = sem("w_low_pool")
        slot_filled = sem("slot_filled")
        products_ready = sem("products_ready")
        diagonals_ready = sem("diagonals_ready")
        diagonals_summed = sem("diagonals_summed")
        products_summed = sem("products_summed")
        z_copied = sem("z_copied")
        h1_filled = sem("h1_filled")
        h1_ready = [sem("h1_ready_act"), sem("h1_ready_dve")]
        h2_filled = sem("h2_filled")
        h2_ready = [sem("h2_ready_act"), sem("h2_ready_dve")]
        y_filled = sem("y_filled")
        y_ready = sem("y_ready")
        y_stored = sem("y_stored")

        def tile_summed(t):
            return 1 + max(q for (m, i), q in product_at.items() if lane_of(i, m) // 32 == t)

        FILLS = len(slot_at)

        def wait_split(engine, *step):
            engine.wait_ge(w_low_pool if by_pool(step) else w_low_vector, low_at[step] + 1)

        def wait_rows_split(engine, g, c):
            if c < chunks_of(2 * g + 1):
                wait_split(engine, "weights", first_chunk(2 * g + 1) + c)
            if c == g:
                wait_split(engine, "diagonals", g)

        def wait_group_split(engine, g):
            wait_rows_split(engine, g, g)

        def raw_chunk(m, c):
            g = m // 2
            rows = min(4, 2 * m - 4 * c)
            j = 2 * (m % 2)
            return raw[g % 2][:, 4 * c:4 * c + rows, j:j + 2, :], rows

        def raw_diagonals(g):
            flat = raw[g % 2][:].rearrange("p i j l -> p (i j) l")
            return flat[:, 16 * g + 1:16 * g + 12:10, :]

        W1_LOADS = 2 + MS + sum(
            1 + (lane_of(i, MS - 1) + 1) // 32 - lane_of(i, i // 2 + 1) // 32 for i in range(FIELDS - 2))

        def low_part(engine, c):
            src, rows = raw_chunk(*chunks[c])
            low, high = (x[:, c % SPLIT_RING, 0:rows, :].rearrange("p i (j l) -> p i j l", j=2)
                         for x in (w_low, w_high[:].bitcast(F32)))
            return engine.tensor_tensor(low, src, high, ALU.subtract)

        block = ctx.enter_context(nc.Block())

        @block.sync
        def _(sp):
            sp.dma_start(ids_sb[:], ids.rearrange("(t p) f -> p t f", p=P)).then_inc(ids_loaded, 16)

            def load_raw(g, c):
                for i in range(4 * c, min(4 * c + 4, 4 * g + 3)):
                    j = max(4 * g, i + 1)
                    k = 4 * g + 4 - j
                    src = w[pair(i, j):pair(i, j) + k, :, :].rearrange("p k l -> k p l")
                    for half in range(1 if c < g else 2):
                        sp.dma_start(raw[g % 2][64 * half:64 * half + 64, i, 4 - k:4, :], src
                                     ).then_inc(raw_loaded[g % 2][c], 16)

            def copy_raw(g, c):
                if c < g:
                    sp.wait_ge(raw_loaded[g % 2][c], 16 * (loads_of(g, c) - 1))
                    sp.dma_start(raw[g % 2][64:128, 4 * c:4 * c + 4, :, :],
                                 raw[g % 2][0:64, 4 * c:4 * c + 4, :, :]).then_inc(raw_loaded[g % 2][c], 16)

            before = None
            for g in range(GS):
                for c in range(g + 1):
                    if g >= 2 and c < g - 1:
                        wait_rows_split(sp, g - 2, c)
                    load_raw(g, c)
                    if before:
                        copy_raw(*before)
                    before = g, c

            wait_group_split(sp, GS - 2)
            sp.dma_start(w2_sb, W_top2.rearrange("(t p) n -> p t n", p=P)).then_inc(w1_loaded, 16)
            n = 1
            for i in range(FIELDS - 2):
                lane, row, left = lane_of(i, i // 2 + 1), pair(i, 2 * (i // 2 + 1)), 2 * (MS - 1 - i // 2)
                while left:
                    t, r = lane // 32, lane % 32
                    k = min(left, 32 - r)
                    at = 32 * (i % 4) + r
                    sp.dma_start(w1_sb[at:at + k, t, :], W_top1[row:row + k, :]).then_inc(w1_loaded, 16)
                    lane, row, left, n = lane + k, row + k, left - k, n + 1
            for m in range(MS):
                row = pair(2 * m, 2 * m + 1)
                sp.dma_start(w1_sb[80 + m:81 + m, 3, :], W_top1[row:row + 1, :]).then_inc(w1_loaded, 16)
            sp.dma_start(w1_sb[112:128, 3, :], W_top1[N1 - DENSE:N1, :]).then_inc(w1_loaded, 16)
            assert n + MS + 1 == W1_LOADS
            sp.wait_ge(y_ready, 1)
            sp.dma_start(out.rearrange("(t p) o -> t (p o)", p=P), y_sb[0:P:32, :]).then_inc(y_stored, 16)
            sp.wait_ge(y_stored, 16)

        @block.gpsimd
        def _(pool):
            pool.wait_ge(constants_ready, 3)
            pool.affine_select(out=identity[:], in_=identity[:], compare_op=ALU.not_equal, fill=1.0,
                               base=0, pattern=[[-1, P]], channel_multiplier=1).then_inc(identity_ready, 1)
            pool.wait_ge(ids_loaded, 16)
            for s in STEPS:
                if s[0] == "gather":
                    m, t, f = s[1:]
                    if m >= GATHER_RING and f == t == 0:
                        pool.wait_ge(slot_filled, slot_at["E", m - GATHER_RING] + 1)
                    pool.indirect_dma_start(
                        out=gathered[:, m % GATHER_RING, t, f, :], out_offset=None,
                        in_=tables[2 * m + f],
                        in_offset=bass.IndirectOffsetOnAxis(
                            ap=ids_sb[:, t, 2 * m + f:2 * m + f + 1], axis=0),
                    ).then_inc(fields_gathered[m % GATHER_RING][t], 16)
                elif by_pool(s):
                    c = s[1]
                    pool.wait_ge(w_high_ready, split_at[s] + 1)
                    low_part(nc.gpsimd, c).then_inc(w_low_pool, 1)

        @block.scalar
        def _(act):
            act.wait_ge(dense_cleared, 1)
            act.dma_start(dense_sb[:, :, 16:32], dense_ctx.rearrange("(t p) d -> p t d", p=P)
                          ).then_inc(small_loaded, 16)
            act.dma_start(b1_sb[:], b_top1.rearrange("(t p) -> p t", p=P),
                          allow_slow_non_contiguous=True).then_inc(small_loaded, 16)
            act.dma_start(b2_sb[:], b_top2.rearrange("(t p) -> p t", p=P),
                          allow_slow_non_contiguous=True).then_inc(small_loaded, 16)
            act.dma_start(w3_sb[:], W_top3.rearrange("(t p) o -> p (t o)", p=P),
                          allow_slow_non_contiguous=True).then_inc(small_loaded, 16)

            for s in STEPS:
                if s[0] == "fields":
                    m = s[1]
                    n = slot_at["E", m]
                    act.wait_ge(slot_filled, n + 1)
                    nc.scalar.activation(e_pairs[:, m, :], slots[:, n % SLOTS, :], ACT.Copy)
                    nc.scalar.activation(pair_part[:], slots[:, n % SLOTS, :],
                                         ACT.Copy).then_inc(pair_copied, 1)
                    last = nc.scalar.activation(e_parts[0:64, 2 * m, :], slots[0:64, n % SLOTS, :], ACT.Copy)
                    if 2 * m + 1 < FIELDS - 1:
                        last = nc.scalar.activation(e_parts[64:128, 2 * m + 1, :],
                                                    slots[64:128, n % SLOTS, :], ACT.Copy)
                    last.then_inc(fields_high, 1)
                elif s[0] == "lows":
                    m = s[1]
                    act.wait_ge(pair_split, m + 1)
                    last = nc.scalar.activation(e_parts[64:128, 2 * m, :], pair_part[0:64, :], ACT.Copy)
                    if 2 * m + 1 < FIELDS - 1:
                        last = nc.scalar.activation(e_parts[0:64, 2 * m + 1, :], pair_part[64:128, :],
                                                    ACT.Copy)
                    last.then_inc(fields_low, 1)
                elif s[0] == "weights":
                    c, (m, at) = s[1], chunks[s[1]]
                    act.wait_ge(raw_loaded[m // 2 % 2][at], 16 * loads_of(m // 2, at))
                    if c >= SPLIT_RING:
                        pm, pc = chunks[c - SPLIT_RING]
                        act.wait_ge(slot_filled, slot_at[pm, min(4 * pc + 3, 2 * pm - 1)] + 1)
                    src, rows = raw_chunk(m, at)
                    nc.scalar.activation(
                        w_high[:, c % SPLIT_RING, 0:rows, :].rearrange("p i (j l) -> p i j l", j=2), src,
                        ACT.Copy).then_inc(w_high_ready, 1)
                elif s[0] == "diagonals":
                    g = s[1]
                    act.wait_ge(raw_loaded[g % 2][g], 16 * loads_of(g, g))
                    if g >= 2:
                        act.wait_ge(slot_filled, slot_at["D", 2 * g - 3] + 1)
                    src = raw_diagonals(g).unsqueeze(2).broadcast_to((P, 2, 2, EMBED))
                    nc.scalar.activation(d_high[:, g % 2, :, :, :], src, ACT.Copy).then_inc(w_high_ready, 1)

            wait_group_split(act, GS - 2)
            for t in range(4):
                act.wait_ge(products_summed, tile_summed(t))
                if t == 3:
                    act.wait_ge(diagonals_summed, GS)
                nc.scalar.activation(z_sb[:, t, :], z_ps[:, t, :], ACT.Copy).then_inc(z_copied, 1)
            act.wait_ge(small_loaded, 64)
            for t in (0, 2):
                act.wait_ge(h1_filled, t + 1)
                nc.scalar.activation(h1_sb[:, t, :], slots[:, (FILLS + t) % SLOTS, :], ACT.Relu,
                                     bias=b1_sb[:, t:t + 1]).then_inc(h1_ready[0], 1)
            act.wait_ge(h2_filled, 1)
            nc.scalar.activation(h2_sb[:, 0, :], z_ps[:, 0, :], ACT.Relu,
                                 bias=b2_sb[:, 0:1]).then_inc(h2_ready[0], 1)
            act.wait_ge(y_filled, 1)
            nc.scalar.activation(y_sb, z_ps[:, 2, 0:P], ACT.Copy).then_inc(y_ready, 1)

        @block.vector
        def _(dve):
            nc.vector.memset(dense_sb[:], 0.0).then_inc(dense_cleared, 1)
            nc.vector.memset(selector[:], 0.0).then_inc(constants_ready, 1)
            nc.vector.memset(zero_row, 0.0).then_inc(constants_ready, 1)
            nc.vector.memset(identity[:], 0.0).then_inc(constants_ready, 1)
            dve.wait_ge(constants_ready, 3)
            nc.vector.memset(selector[0:64, 31:32], 1.0).then_inc(constants_ready, 1)
            nc.vector.memset(selector[64:128, 32:33], 1.0).then_inc(constants_ready, 1)

            for s in STEPS:
                if s[0] == "lows":
                    m = s[1]
                    dve.wait_ge(pair_copied, m + 1)
                    nc.vector.tensor_tensor(pair_part[:], e_pairs[:, m, :], pair_part[:].bitcast(F32),
                                            ALU.subtract).then_inc(pair_split, 1)
                elif s[0] == "weights" and not by_pool(s):
                    dve.wait_ge(w_high_ready, split_at[s] + 1)
                    low_part(nc.vector, s[1]).then_inc(w_low_vector, 1)
                elif s[0] == "diagonals":
                    g = s[1]
                    dve.wait_ge(w_high_ready, split_at[s] + 1)
                    src = raw_diagonals(g).unsqueeze(2).broadcast_to((P, 2, 2, EMBED))
                    nc.vector.tensor_tensor(d_low[:, g % 2, :, :, :], src,
                                            d_high[:, g % 2, :, :, :].bitcast(F32),
                                            ALU.subtract).then_inc(w_low_vector, 1)
                elif s[0] == "diagonal":
                    m = s[1]
                    n = slot_at["D", m]
                    if m % 2 == 0 and m >= 4:
                        dve.wait_ge(diagonals_summed, m // 2 - 1)
                    dve.wait_ge(slot_filled, n + 1)
                    half = 64 * (m % 2)
                    nc.vector.tensor_tensor(
                        d_products[half:half + 64, m // 2 % 2, :], slots[64:128, n % SLOTS, :], e_pairs[64:128, m, :],
                        ALU.mult).then_inc(diagonals_ready, 1)
                elif s[0] == "block":
                    m, i = s[1:]
                    n, q = slot_at[m, i], product_at[m, i]
                    if q >= PRODUCT_RING:
                        dve.wait_ge(products_summed, q - PRODUCT_RING + 1)
                    dve.wait_ge(slot_filled, n + 1)
                    nc.vector.tensor_tensor(
                        products[:, q % PRODUCT_RING, :], slots[:, n % SLOTS, :], e_pairs[:, m, :],
                        ALU.mult).then_inc(products_ready, 1)

            dve.wait_ge(small_loaded, 64)
            for t in (1, 3):
                dve.wait_ge(h1_filled, t + 1)
                nc.vector.tensor_scalar(h1_sb[:, t, :], slots[:, (FILLS + t) % SLOTS, :], b1_sb[:, t:t + 1], 0.0,
                                        ALU.add, ALU.max).then_inc(h1_ready[1], 1)
            dve.wait_ge(h2_filled, 2)
            nc.vector.tensor_scalar(h2_sb[:, 1, :], z_ps[:, 1, :], b2_sb[:, 1:2], 0.0,
                                    ALU.add, ALU.max).then_inc(h2_ready[1], 1)

        @block.tensor
        def _(pe):
            pe.wait_ge(constants_ready, 5)
            for t in range(4):
                for q in range(4):
                    nc.tensor.matmul(z_ps[32 * q:32 * q + 32, t, :], zero_row[:, 0:32], zero_row,
                                     start=True, stop=False, skip_group_check=True)
            pe.wait_ge(identity_ready, 1)
            pe.wait_ge(small_loaded, 64)
            for t in range(BT):
                nc.tensor.matmul(z_ps[96:128, 3, P * t:P * t + P], dense_sb[:, t, :], identity[:],
                                 start=False, stop=False, skip_group_check=True)

            def free_slot(n):
                if n >= SLOTS:
                    before = by_slot[n - SLOTS]
                    if before[0] == "E":
                        pe.wait_ge(fields_high, before[1] + 1)
                    elif before[0] == "D":
                        pe.wait_ge(diagonals_ready, before[1] + 1)
                    else:
                        pe.wait_ge(products_ready, product_at[before] + 1)

            def sum_over_l(quadrant, lane, of, last):
                t, r = lane // 32, lane % 32
                return nc.tensor.matmul(z_ps[32 * quadrant:32 * quadrant + 32, t, :],
                                        selector[:, 31 - r:63 - r], of, start=False, stop=last,
                                        skip_group_check=True)

            def sum_batch(batch):
                m = batch[0][0]
                pe.wait_ge(products_ready, product_at[batch[-1]] + 1)
                for _, i in batch:
                    summed = sum_over_l(i % 4, lane_of(i, m), products[:, product_at[m, i] % PRODUCT_RING, :],
                                        m == MS - 1)
                summed.then_inc(products_summed, len(batch))
                if m % 2 and batch[-1][1] == 2 * m - 1:
                    g = m // 2
                    pe.wait_ge(diagonals_ready, 2 * g + 2)
                    sum_over_l(2, 96 + DENSE + 2 * g, d_products[:, g % 2, :], g == GS - 1
                               ).then_inc(diagonals_summed, 1)

            unsummed = sum_batches()
            for s in STEPS:
                if s[0] == "fields":
                    m = s[1]
                    n = slot_at["E", m]
                    free_slot(n)
                    for t in range(BT):
                        pe.wait_ge(fields_gathered[m % GATHER_RING][t], 16 * 2 * (m // GATHER_RING + 1))
                        last = nc.tensor.transpose(
                            slots[:, n % SLOTS, P * t:P * t + P],
                            gathered[:, m % GATHER_RING, t, :, :].rearrange("p f k -> p (f k)"), identity[:])
                    last.then_inc(slot_filled, 1)
                elif s[0] == "diagonal":
                    m = s[1]
                    n = slot_at["D", m]
                    pe.wait_ge(fields_low, m + 1)
                    wait_split(pe, "diagonals", m // 2)
                    free_slot(n)
                    for part, weights in enumerate((d_high, d_low)):
                        last = nc.tensor.matmul(
                            slots[:, n % SLOTS, :],
                            weights[:, m // 2 % 2, m % 2, :, :].rearrange("p c l -> p (c l)"),
                            e_parts[:, 2 * m, :], start=part == 0, stop=part == 1)
                    last.then_inc(slot_filled, 1)
                elif s[0] == "block":
                    m, i = s[1:]
                    n, q = slot_at[m, i], product_at[m, i]
                    c = first_chunk(m) + i // 4
                    if i % 4 == 0:
                        wait_split(pe, "weights", c)
                    free_slot(n)
                    for part, weights in enumerate((w_high, w_low)):
                        last = nc.tensor.matmul(slots[:, n % SLOTS, :], weights[:, c % SPLIT_RING, i % 4, :],
                                                e_parts[:, i, :], start=part == 0, stop=part == 1)
                    last.then_inc(slot_filled, 1)
                    if q >= product_at[unsummed[0][-1]] + SUM_LAG:
                        sum_batch(unsummed.pop(0))

            def dense_1(n, k):
                return nc.tensor.matmul(slots[:, (FILLS + n) % SLOTS, :], w1_sb[:, k, P * n:P * n + P],
                                        z_sb[:, k, :], start=k == 0, stop=k == 3, skip_group_check=True)

            def dense_2(n, k):
                return nc.tensor.matmul(z_ps[:, n, :], w2_sb[:, k, P * n:P * n + P], h1_sb[:, k, :],
                                        start=k == 0, stop=k == 3, skip_group_check=True)

            pe.wait_ge(w1_loaded, 16 * W1_LOADS)
            for n in range(N1 // P):
                free_slot(FILLS + n)
                for k in range(3):
                    if n == 0:
                        pe.wait_ge(z_copied, k + 1)
                    dense_1(n, k)
                if n == 0:
                    for batch in unsummed:
                        sum_batch(batch)
            pe.wait_ge(z_copied, 4)
            for n in range(N1 // P):
                dense_1(n, 3).then_inc(h1_filled, 1)
            for k in range(3):
                pe.wait_ge(h1_ready[k % 2], k // 2 + 1)
                for n in range(N2 // P):
                    dense_2(n, k)
            pe.wait_ge(h1_ready[1], 2)
            for n in range(N2 // P):
                dense_2(n, 3).then_inc(h2_filled, 1)
            for k in range(N2 // P):
                pe.wait_ge(h2_ready[k % 2], 1)
                for t in range(BT):
                    last = nc.tensor.matmul(z_ps[32 * t:32 * t + 1, 2, 0:P], w3_sb[:, k:k + 1],
                                            h2_sb[:, k, P * t:P * t + P], start=k == 0, stop=k == 1,
                                            skip_group_check=True)
            last.then_inc(y_filled, 1)


def kernel(**inputs):
    import numpy as np
    import concourse.bacc as bacc
    from concourse.bass_utils import run_bass_kernel_spmd

    nc = bacc.Bacc("TRN2", target_bir_lowering=False, num_devices=1)
    arrays, aps = {}, {}
    for name, value in inputs.items():
        a = np.ascontiguousarray(value)
        arrays[f"in_{name}"] = a
        aps[name] = nc.dram_tensor(f"in_{name}", a.shape, mybir.dt.from_np(a.dtype),
                                   kind="ExternalInput").ap()
    out = nc.dram_tensor("out_y", (BATCH, 1), F32, kind="ExternalOutput").ap()
    dlrm_tower(nc, aps["dense_ctx"], aps["ids"], [aps[f"tbl_{f}"] for f in range(FIELDS)],
               aps["W_top1"], aps["b_top1"], aps["W_top2"], aps["b_top2"], aps["W_top3"],
               aps["L0_rec_w"], out)
    r = run_bass_kernel_spmd(nc, [arrays], core_ids=[0])
    return r.results[0]["out_y"]
```
